# Optimizing a Trainium2 kernel written in Bass

```python
import numpy as np
import jax
import jax.numpy as jnp

def _softmax(x, axis=-1):
    return jax.nn.softmax(x, axis=axis)

def _gelu(x):
    return jax.nn.gelu(x, approximate=True)

def _silu(x):
    return jax.nn.silu(x)

def _sigmoid(x):
    return jax.nn.sigmoid(x)

def _layernorm(x, axis=-1, eps=1e-05):
    m = jnp.mean(x, axis=axis, keepdims=True)
    v = jnp.var(x, axis=axis, keepdims=True)
    return (x - m) / jnp.sqrt(v + eps)

def _scatter_add(tgt, idx, src, axis=0):
    return tgt.at[idx].add(src)

def _segment_sum(src, seg, n):
    return jax.ops.segment_sum(src, seg, n)
kernel_name = 'mk_dlrm_tower_d1_rec_r8_4da8f4'

def setup_inputs(seed: int=0):
    np.random.seed(seed)
    _w = jnp.asarray

    def _rec_inputs():
        import jax
        import jax.numpy as jnp
        _tk = jax.random.key(seed)
        ids = jnp.stack([jax.random.randint(jax.random.fold_in(_tk, 200 + f), (512,), 0, v, jnp.int32) for f, v in enumerate([12500, 1250, 12500, 1000, 1250, 1250, 1000, 1250, 12500, 12500, 1250, 12500, 125000, 1250, 1250, 1000, 1250, 1250, 1000, 1000, 12500, 1250, 1250, 12500, 12500, 1000])], axis=1)
        tbl_0 = 0.05 * jax.random.normal(jax.random.fold_in(_tk, 500 + 0), (12500, 128), jnp.float32)
        tbl_1 = 0.05 * jax.random.normal(jax.random.fold_in(_tk, 500 + 1), (1250, 128), jnp.float32)
        tbl_2 = 0.05 * jax.random.normal(jax.random.fold_in(_tk, 500 + 2), (12500, 128), jnp.float32)
        tbl_3 = 0.05 * jax.random.normal(jax.random.fold_in(_tk, 500 + 3), (1000, 128), jnp.float32)
        tbl_4 = 0.05 * jax.random.normal(jax.random.fold_in(_tk, 500 + 4), (1250, 128), jnp.float32)
        tbl_5 = 0.05 * jax.random.normal(jax.random.fold_in(_tk, 500 + 5), (1250, 128), jnp.float32)
        tbl_6 = 0.05 * jax.random.normal(jax.random.fold_in(_tk, 500 + 6), (1000, 128), jnp.float32)
        tbl_7 = 0.05 * jax.random.normal(jax.random.fold_in(_tk, 500 + 7), (1250, 128), jnp.float32)
        tbl_8 = 0.05 * jax.random.normal(jax.random.fold_in(_tk, 500 + 8), (12500, 128), jnp.float32)
        tbl_9 = 0.05 * jax.random.normal(jax.random.fold_in(_tk, 500 + 9), (12500, 128), jnp.float32)
        tbl_10 = 0.05 * jax.random.normal(jax.random.fold_in(_tk, 500 + 10), (1250, 128), jnp.float32)
        tbl_11 = 0.05 * jax.random.normal(jax.random.fold_in(_tk, 500 + 11), (12500, 128), jnp.float32)
        tbl_12 = 0.05 * jax.random.normal(jax.random.fold_in(_tk, 500 + 12), (125000, 128), jnp.float32)
        tbl_13 = 0.05 * jax.random.normal(jax.random.fold_in(_tk, 500 + 13), (1250, 128), jnp.float32)
        tbl_14 = 0.05 * jax.random.normal(jax.random.fold_in(_tk, 500 + 14), (1250, 128), jnp.float32)
        tbl_15 = 0.05 * jax.random.normal(jax.random.fold_in(_tk, 500 + 15), (1000, 128), jnp.float32)
        tbl_16 = 0.05 * jax.random.normal(jax.random.fold_in(_tk, 500 + 16), (1250, 128), jnp.float32)
        tbl_17 = 0.05 * jax.random.normal(jax.random.fold_in(_tk, 500 + 17), (1250, 128), jnp.float32)
        tbl_18 = 0.05 * jax.random.normal(jax.random.fold_in(_tk, 500 + 18), (1000, 128), jnp.float32)
        tbl_19 = 0.05 * jax.random.normal(jax.random.fold_in(_tk, 500 + 19), (1000, 128), jnp.float32)
        tbl_20 = 0.05 * jax.random.normal(jax.random.fold_in(_tk, 500 + 20), (12500, 128), jnp.float32)
        tbl_21 = 0.05 * jax.random.normal(jax.random.fold_in(_tk, 500 + 21), (1250, 128), jnp.float32)
        tbl_22 = 0.05 * jax.random.normal(jax.random.fold_in(_tk, 500 + 22), (1250, 128), jnp.float32)
        tbl_23 = 0.05 * jax.random.normal(jax.random.fold_in(_tk, 500 + 23), (12500, 128), jnp.float32)
        tbl_24 = 0.05 * jax.random.normal(jax.random.fold_in(_tk, 500 + 24), (12500, 128), jnp.float32)
        tbl_25 = 0.05 * jax.random.normal(jax.random.fold_in(_tk, 500 + 25), (1000, 128), jnp.float32)
        _rk = jax.random.fold_in(_tk, 7)
        r_dense_features = -0.000520686 + 1.00062 * jax.random.normal(jax.random.fold_in(_rk, 101), (512, 128), jnp.float32)
        W_top1 = 0.0405887 * jax.random.normal(jax.random.fold_in(_tk, 801), (607, 512), jnp.float32)
        W_top2 = 0.0441942 * jax.random.normal(jax.random.fold_in(_tk, 802), (512, 256), jnp.float32)
        W_top3 = 0.0625 * jax.random.normal(jax.random.fold_in(_tk, 803), (256, 1), jnp.float32)
        b_top1 = jnp.zeros((512,), jnp.float32)
        b_top2 = jnp.zeros((256,), jnp.float32)
        return (r_dense_features, ids, tbl_0, tbl_1, tbl_2, tbl_3, tbl_4, tbl_5, tbl_6, tbl_7, tbl_8, tbl_9, tbl_10, tbl_11, tbl_12, tbl_13, tbl_14, tbl_15, tbl_16, tbl_17, tbl_18, tbl_19, tbl_20, tbl_21, tbl_22, tbl_23, tbl_24, tbl_25, W_top1, b_top1, W_top2, b_top2, W_top3)
    r_dense_features, ids, tbl_0, tbl_1, tbl_2, tbl_3, tbl_4, tbl_5, tbl_6, tbl_7, tbl_8, tbl_9, tbl_10, tbl_11, tbl_12, tbl_13, tbl_14, tbl_15, tbl_16, tbl_17, tbl_18, tbl_19, tbl_20, tbl_21, tbl_22, tbl_23, tbl_24, tbl_25, W_top1, b_top1, W_top2, b_top2, W_top3 = _rec_inputs()

    def _L0_rec_setup():
        import jax, jax.numpy as jnp
        import numpy as np
        NUM_SPARSE = 26
        EMBED_DIM = 128
        BATCH = 2048
        key = jax.random.key(seed)
        k1, k2 = jax.random.split(key)
        dense_features = jax.random.normal(k1, (BATCH, EMBED_DIM), dtype=jnp.float32)
        sparse_features = jax.random.normal(k2, (BATCH, NUM_SPARSE, EMBED_DIM), dtype=jnp.float32)
        return {'dense_features': dense_features, 'sparse_features': sparse_features}
    _L0_rec_all = _L0_rec_setup()
    _L0_rec_in = {k: v for k, v in _L0_rec_all.items() if k in ()}
    del _L0_rec_all
    return {'r_dense_features': r_dense_features, 'ids': ids, 'tbl_0': tbl_0, 'tbl_1': tbl_1, 'tbl_2': tbl_2, 'tbl_3': tbl_3, 'tbl_4': tbl_4, 'tbl_5': tbl_5, 'tbl_6': tbl_6, 'tbl_7': tbl_7, 'tbl_8': tbl_8, 'tbl_9': tbl_9, 'tbl_10': tbl_10, 'tbl_11': tbl_11, 'tbl_12': tbl_12, 'tbl_13': tbl_13, 'tbl_14': tbl_14, 'tbl_15': tbl_15, 'tbl_16': tbl_16, 'tbl_17': tbl_17, 'tbl_18': tbl_18, 'tbl_19': tbl_19, 'tbl_20': tbl_20, 'tbl_21': tbl_21, 'tbl_22': tbl_22, 'tbl_23': tbl_23, 'tbl_24': tbl_24, 'tbl_25': tbl_25, 'W_top1': W_top1, 'b_top1': b_top1, 'W_top2': W_top2, 'b_top2': b_top2, 'W_top3': W_top3}

def reference(r_dense_features, ids, tbl_0, tbl_1, tbl_2, tbl_3, tbl_4, tbl_5, tbl_6, tbl_7, tbl_8, tbl_9, tbl_10, tbl_11, tbl_12, tbl_13, tbl_14, tbl_15, tbl_16, tbl_17, tbl_18, tbl_19, tbl_20, tbl_21, tbl_22, tbl_23, tbl_24, tbl_25, W_top1, b_top1, W_top2, b_top2, W_top3):
    import jax
    import jax.numpy as jnp

    def _L0_rec_ref(dense_features, sparse_features):
        import jax, jax.numpy as jnp
        import numpy as np
        NUM_SPARSE = 26
        EMBED_DIM = 128
        BATCH = 2048
        F = NUM_SPARSE + 1
        combined = jnp.concatenate([dense_features[:, None, :], sparse_features], axis=1)
        interactions = jnp.einsum('bfd,bgd->bfg', combined, combined)
        iu, ju = jnp.triu_indices(F, k=1)
        interactions_flat = interactions[:, iu, ju]
        return jnp.concatenate([dense_features, interactions_flat], axis=1)
    e = jnp.stack([tbl_0[ids[:, 0]], tbl_1[ids[:, 1]], tbl_2[ids[:, 2]], tbl_3[ids[:, 3]], tbl_4[ids[:, 4]], tbl_5[ids[:, 5]], tbl_6[ids[:, 6]], tbl_7[ids[:, 7]], tbl_8[ids[:, 8]], tbl_9[ids[:, 9]], tbl_10[ids[:, 10]], tbl_11[ids[:, 11]], tbl_12[ids[:, 12]], tbl_13[ids[:, 13]], tbl_14[ids[:, 14]], tbl_15[ids[:, 15]], tbl_16[ids[:, 16]], tbl_17[ids[:, 17]], tbl_18[ids[:, 18]], tbl_19[ids[:, 19]], tbl_20[ids[:, 20]], tbl_21[ids[:, 21]], tbl_22[ids[:, 22]], tbl_23[ids[:, 23]], tbl_24[ids[:, 24]], tbl_25[ids[:, 25]]], axis=1)
    z = _L0_rec_ref(r_dense_features, e)
    z = z.reshape(z.shape[0], -1)
    h = jnp.concatenate([z, r_dense_features], axis=1)
    h = jnp.maximum(h @ W_top1 + b_top1, 0.0)
    h = jnp.maximum(h @ W_top2 + b_top2, 0.0)
    y = h @ W_top3
    return y

_drawn_inputs = setup_inputs


def setup_inputs(seed=0):
    import zlib

    import numpy as np

    out = dict(_drawn_inputs(seed))
    spreads = {'b_top1': (0.0, 0.1), 'b_top2': (0.0, 0.1)}
    factors = {}
    for name, (base, spread) in spreads.items():
        noise = np.random.default_rng([zlib.crc32(name.encode()), seed]).standard_normal(out[name].shape)
        drawn = base * np.exp(spread * noise) if base else spread * noise
        out[name] = jnp.asarray(drawn.astype(out[name].dtype))
    for name, factor in factors.items():
        out[name] = (out[name] * factor).astype(out[name].dtype)
    return out
```

```python
import concourse.bass as bass
from concourse import mybir
from contextlib import ExitStack

F32 = mybir.dt.float32
BF16 = mybir.dt.bfloat16
I32 = mybir.dt.int32
U32 = mybir.dt.uint32
ALU = mybir.AluOpType
ACT = mybir.ActivationFunctionType

P = 128
BATCH = 512
EMBED = 128
TABLE_ROWS = [12500, 1250, 12500, 1000, 1250, 1250, 1000, 1250, 12500, 12500, 1250, 12500, 125000,
              1250, 1250, 1000, 1250, 1250, 1000, 1000, 12500, 1250, 1250, 12500, 12500, 1000]
SPARSE = len(TABLE_ROWS)
FEATURES = SPARSE + 1
HIDDEN1 = 512
HIDDEN2 = 256
TILE = 128
TILES = BATCH // TILE
HALF = TILE // 2
HOT = 4
HOT_ROWS = min(TABLE_ROWS)
HOT_TABLES = [f for f in range(SPARSE) if TABLE_ROWS[f] == HOT_ROWS][:HOT]
COLD_TABLES = [f for f in range(SPARSE) if f not in HOT_TABLES]
HOT_BLOCKS = -(-HOT_ROWS // P)
HOT_SPAN = HOT_BLOCKS * P
SPLITS = 3
KEPT = 1 + HOT
GATHERS = len(COLD_TABLES) * HALF // P
PER_GATHER = P // HALF
SLOTS = 32
QUAD = 4
UNITS = 2
UNIT = HALF // UNITS
QUADS = UNIT // QUAD
COLS = FEATURES - 1
PAIR_TILES = -(-COLS // QUAD)
N1 = HIDDEN1 // P
N2 = HIDDEN2 // P
BANK = 512
GROUPS = [range(g, min(g + BANK // P, GATHERS)) for g in range(0, GATHERS, BANK // P)]

HOT_ORDER = sorted(((k, i) for k in range(HOT) for i in range(SPLITS)), key=lambda ki: (ki[0] + 2 * ki[1], ki[1]))


def dlrm_tower(nc, table, numbers, hot_tables, hot_ids, dense_t, identity, w_pairs,
               w_dense_a, w_dense_b, b_top1, w_top2, b_top2, w_top3, out):
    with ExitStack() as ctx:
        def sbuf(name, shape, dtype=F32):
            return ctx.enter_context(nc.sbuf_tensor(name, shape, dtype))

        def psum(name, columns):
            return ctx.enter_context(nc.psum_tensor(name, [P, columns], F32))

        def sem(name):
            return ctx.enter_context(nc.semaphore(name))

        numbers_sb = sbuf("numbers_sb", [P, (TILES * 2 + 1) * GATHERS + HOT_BLOCKS], I32)
        rows = sbuf("rows", [P, TILES * 2, GATHERS], I32)
        hot_ids_sb = sbuf("hot_ids_sb", [P, TILES, HOT, TILE], I32)
        hot_rest = sbuf("hot_rest", [P, HOT, HOT_BLOCKS, EMBED])
        hot_split = [sbuf(f"hot_split{i}", [P, HOT, HOT_BLOCKS, EMBED], BF16) for i in range(SPLITS)]
        one_hot = sbuf("one_hot", [P, HOT, HOT_BLOCKS, TILE], BF16)
        kept = sbuf("kept", [P, KEPT, BATCH])
        gathered = [sbuf(f"gathered{h}", [P, GATHERS, EMBED]) for h in range(2)]
        features_t = [sbuf(f"features_t{h}", [P, HALF, SLOTS]) for h in range(2)]
        ident_sb = sbuf("ident_sb", [P, P])
        pairs = sbuf("pairs", [P, PAIR_TILES, TILE])
        w_pairs_sb = sbuf("w_pairs_sb", [P, PAIR_TILES, HIDDEN1])
        w_dense_in = sbuf("w_dense_in", [P, 2, HIDDEN1])
        w_dense = sbuf("w_dense", [P, HIDDEN1])
        w2_sb = sbuf("w2_sb", [P, N1, HIDDEN2])
        w3_sb = sbuf("w3_sb", [P, N2])
        b1_sb = sbuf("b1_sb", [P, N1])
        b2_sb = sbuf("b2_sb", [P, N2])
        h1 = sbuf("h1", [P, N1, TILE])
        h2 = sbuf("h2", [P, N2, TILE])
        y_row = sbuf("y_row", [1, BATCH])

        ps_turn = [psum(f"ps_turn{k}", BANK) for k in range(2)]
        ps_gram = [psum(f"ps_gram{u}", QUADS * P) for u in range(UNITS)]
        ps_mlp = [psum(f"ps_mlp{k}", BANK) for k in range(2)]

        numbers_loaded = sem("numbers_loaded")
        hot_ids_loaded = [sem(f"hot_ids_loaded{i}") for i in range(3)]
        hot_loaded = [sem(f"hot_loaded{k}") for k in range(HOT)]
        dense_loaded = sem("dense_loaded")
        ident_loaded = sem("ident_loaded")
        w_dense_loaded = sem("w_dense_loaded")
        w1_loaded = sem("w1_loaded")
        w2_loaded = sem("w2_loaded")
        bias_loaded = sem("bias_loaded")
        slots_zeroed = sem("slots_zeroed")
        w_dense_ready = sem("w_dense_ready")
        rows_ready = sem("rows_ready")
        rest_ready = sem("rest_ready")
        split_ready = [sem(f"split_ready{i}") for i in range(SPLITS)]
        one_hot_ready = sem("one_hot_ready")
        hot_read = sem("hot_read")
        hot_kept = sem("hot_kept")
        arrived = [[sem(f"arrived{h}_{g}") for g in range(len(GROUPS))] for h in range(2)]
        turned = [sem(f"turned{h}") for h in range(2)]
        kept_placed = sem("kept_placed")
        placed_dve = sem("placed_dve")
        placed_act = sem("placed_act")
        gram_done = [sem(f"gram_done{u}") for u in range(UNITS)]
        pairs_dve = [sem(f"pairs_dve{u}") for u in range(UNITS)]
        pairs_act = [sem(f"pairs_act{u}") for u in range(UNITS)]
        h1_sum = [sem(f"h1_sum{k}") for k in range(2)]
        h1_ready = [sem(f"h1_ready{k}") for k in range(2)]
        h2_sum = [sem(f"h2_sum{k}") for k in range(2)]
        h2_ready = [sem(f"h2_ready{k}") for k in range(2)]
        y_sum = sem("y_sum")
        y_ready = sem("y_ready")
        stored = sem("stored")

        ids_sb = numbers_sb[:, 0:TILES * 2 * GATHERS].rearrange("p (h k) -> p h k", k=GATHERS)
        base_sb = numbers_sb[:, TILES * 2 * GATHERS:(TILES * 2 + 1) * GATHERS]
        hot_row_sb = numbers_sb[:, (TILES * 2 + 1) * GATHERS:]

        block = ctx.enter_context(nc.Block())
        last_tile = TILES - 1

        def number(h, g):
            return h * len(GROUPS) + g

        def is_last(t):
            return isinstance(t, int) and t == last_tile

        def reused(engine, semaphore, uses):
            if not (isinstance(uses, int) and uses == 0):
                engine.wait_ge(semaphore, uses)

        def place_group(copy, h, g):
            first, n = PER_GATHER * GROUPS[g][0], PER_GATHER * len(GROUPS[g])
            return copy(features_t[h][:, :, KEPT + first:KEPT + first + n],
                        ps_turn[number(h, g) % 2][:, 0:n * HALF].rearrange("p (f s) -> p s f", s=HALF))

        def place_pairs(copy, h, u, samples):
            for j in samples:
                for j2 in range(QUAD):
                    n = len(range(j2, COLS, QUAD))
                    at = h * HALF + u * UNIT + j
                    dst = pairs[32 * j2:32 * j2 + 32, 0:n, at:at + UNIT - QUAD + 1:QUAD]
                    src = ps_gram[u][32 * j:32 * j + 32, :].rearrange("p (i c) -> p i c", c=P)
                    c = j * COLS + j2
                    last = copy(dst.rearrange("p q i -> p i q"), src[:, :, c:c + QUAD * (n - 1) + 1:QUAD])
            return last

        @block.sync
        def _(sp):
            sp.dma_start(numbers_sb[:, :], numbers).then_inc(numbers_loaded, 16)
            for k in range(HOT):
                sp.dma_start(hot_rest[:, k], hot_tables[k]).then_inc(hot_loaded[k], 16)
            sp.dma_start(hot_ids_sb[:, 1], hot_ids[:, 1]).then_inc(hot_ids_loaded[1], 16)
            sp.wait_ge(turned[0], len(GROUPS))
            sp.dma_start(w_dense_in[:, 0, :], w_dense_a).then_inc(w_dense_loaded, 16)
            sp.dma_start(w_dense_in[:, 1, :], w_dense_b).then_inc(w_dense_loaded, 16)
            for q in range(PAIR_TILES):
                if q == PAIR_TILES // 2:
                    sp.wait_ge(turned[1], 1)
                sp.dma_start(w_pairs_sb[:, q, :], w_pairs[:, q]).then_inc(w1_loaded, 16)
            sp.wait_ge(turned[1], len(GROUPS))
            sp.dma_start(b1_sb[:, :], b_top1).then_inc(bias_loaded, 16)
            sp.dma_start(b2_sb[:, :], b_top2).then_inc(bias_loaded, 16)
            sp.dma_start(w2_sb[:, :, :], w_top2).then_inc(w2_loaded, 16)
            sp.dma_start(w3_sb[:, :], w_top3).then_inc(w2_loaded, 16)
            sp.dma_start(hot_ids_sb[:, 2:TILES], hot_ids[:, 2:TILES]).then_inc(hot_ids_loaded[2], 16)
            sp.wait_ge(y_ready, TILES)
            sp.dma_start(out, y_row[:, :]).then_inc(stored, 16)
            sp.wait_ge(stored, 16)

        @block.gpsimd
        def _(pool):
            pool.wait_ge(rows_ready, 1)
            for t in range(TILES):
                for h in range(2):
                    for g, group in enumerate(GROUPS):
                        if t >= 1:
                            pool.wait_ge(turned[h], (t - 1) * len(GROUPS) + g + 1)
                        for k in group:
                            pool.indirect_dma_start(
                                out=gathered[h][:, k, :], out_offset=None, in_=table,
                                in_offset=bass.IndirectOffsetOnAxis(
                                    ap=rows[:, 2 * t + h, k:k + 1].bitcast(U32), axis=0),
                            ).then_inc(arrived[h][g], 16)

        @block.tensor
        def _(pe):
            def read_hot(t, k, i):
                if i == 0:
                    pe.wait_ge(one_hot_ready, t * HOT + k + 1)
                if isinstance(t, int) and t == 0:
                    pe.wait_ge(split_ready[i], k + 1)
                for b in range(HOT_BLOCKS):
                    last = nc.tensor.matmul(
                        ps_mlp[1][:, k * TILE:(k + 1) * TILE], hot_split[i][:, k, b, :], one_hot[:, k, b, :],
                        start=(k == 0 and i == 0 and b == 0),
                        stop=(i == SPLITS - 1 and b == HOT_BLOCKS - 1), skip_group_check=True)
                if k == HOT - 1 and i == SPLITS - 1:
                    last.then_inc(hot_read, 1)

            def read_hot_tables(t, tables):
                for k in tables:
                    for i in range(SPLITS):
                        read_hot(t, k, i)

            def turn(t, h, g):
                group, n = GROUPS[g], number(h, g)
                pe.wait_ge(arrived[h][g], (t + 1) * (16 * len(group)))
                reused(pe, (placed_dve, placed_act)[n % 2], t * len(GROUPS) + n // 2)
                for i, k in enumerate(group):
                    last = nc.tensor.transpose(ps_turn[n % 2][:, i * P:(i + 1) * P],
                                               gathered[h][:, k, :], ident_sb[:, :])
                last.then_inc(turned[h], 1)

            def gram(t, h):
                n = (h + 1) * len(GROUPS)
                pe.wait_ge(placed_dve, t * len(GROUPS) + (n + 1) // 2)
                pe.wait_ge(placed_act, t * len(GROUPS) + n // 2)
                pe.wait_ge(kept_placed, t * 2 + h + 1)
                for u in range(UNITS):
                    reused(pe, pairs_dve[u], t * 2 + h)
                    reused(pe, pairs_act[u], t * 2 + h)
                    for i in range(QUADS):
                        s = u * UNIT + i * QUAD
                        last = nc.tensor.matmul(
                            ps_gram[u][:, i * P:i * P + QUAD * COLS],
                            features_t[h][:, s:s + QUAD, :].rearrange("p s f -> p (s f)"),
                            features_t[h][:, s:s + QUAD, 1:FEATURES], start=True, stop=True)
                    last.then_inc(gram_done[u], 1)

            def first_layer_dense(t, k):
                if k == 0:
                    reused(pe, y_ready, t)
                else:
                    pe.wait_ge(hot_kept, t + 2 if not is_last(t) else t + 1)
                for n in range(N1 // 2):
                    hidden = (k * N1 // 2 + n) * P
                    nc.tensor.matmul(ps_mlp[k][:, n * TILE:(n + 1) * TILE], w_dense[:, hidden:hidden + P],
                                     kept[:, 0, bass.ds(t * TILE, TILE)],
                                     start=(n == 0), stop=False, skip_group_check=True)

            def first_layer_pairs(t, k):
                if k == 0:
                    pe.wait_ge(pairs_dve[UNITS - 1], t * 2 + 2)
                    pe.wait_ge(pairs_act[UNITS - 1], t * 2 + 2)
                for n in range(N1 // 2):
                    hidden = (k * N1 // 2 + n) * P
                    for q in range(PAIR_TILES):
                        last = nc.tensor.matmul(
                            ps_mlp[k][:, n * TILE:(n + 1) * TILE], w_pairs_sb[:, q, hidden:hidden + P],
                            pairs[:, q, :], start=False, stop=(q == PAIR_TILES - 1), skip_group_check=True)
                last.then_inc(h1_sum[k], 1)

            def second_layer(t):
                pe.wait_ge(h1_ready[0], t + 1)
                for n in range(N2):
                    for k in range(N1):
                        if n == 0 and k == N1 // 2:
                            pe.wait_ge(h1_ready[1], t + 1)
                        last = nc.tensor.matmul(ps_mlp[n][:, 0:TILE], w2_sb[:, k, n * P:(n + 1) * P], h1[:, k, :],
                                                start=(k == 0), stop=(k == N1 - 1))
                    last.then_inc(h2_sum[n], 1)

            def third_layer(t):
                pe.wait_ge(h2_ready[0], t + 1)
                pe.wait_ge(h2_ready[1], t + 1)
                for k in range(N2):
                    last = nc.tensor.matmul(ps_mlp[0][0:1, 0:TILE], w3_sb[:, k:k + 1], h2[:, k, :],
                                            start=(k == 0), stop=(k == N2 - 1))
                last.then_inc(y_sum, 1)

            def tile(t):
                turn(t, 0, 0)
                turn(t, 0, 1)
                first_layer_dense(t - 1, 0)
                first_layer_pairs(t - 1, 0)
                turn(t, 0, 2)
                first_layer_dense(t - 1, 1)
                first_layer_pairs(t - 1, 1)
                gram(t, 0)
                turn(t, 1, 0)
                second_layer(t - 1)
                turn(t, 1, 1)
                third_layer(t - 1)
                if not is_last(t):
                    read_hot_tables(t + 1, range(HOT // 2))
                turn(t, 1, 2)
                if not is_last(t):
                    read_hot_tables(t + 1, range(HOT // 2, HOT))
                gram(t, 1)

            pe.wait_ge(ident_loaded, 16)
            for g in range(len(GROUPS)):
                for k, i in HOT_ORDER[g * len(HOT_ORDER) // 3:(g + 1) * len(HOT_ORDER) // 3]:
                    read_hot(0, k, i)
                turn(0, 0, g)
            pe.wait_ge(slots_zeroed, 3)
            gram(0, 0)
            turn(0, 1, 0)
            read_hot_tables(1, [0])
            turn(0, 1, 1)
            read_hot_tables(1, [1])
            turn(0, 1, 2)
            read_hot_tables(1, range(2, HOT))
            gram(0, 1)
            pe.wait_ge(w_dense_ready, 1)
            pe.wait_ge(w1_loaded, 16 * PAIR_TILES)
            pe.wait_ge(w2_loaded, 32)
            pe.wait_ge(dense_loaded, 16)
            with pe.Fori(1, last_tile) as t:
                tile(t)
            tile(last_tile)
            for k in range(2):
                first_layer_dense(last_tile, k)
            for k in range(2):
                first_layer_pairs(last_tile, k)
            second_layer(last_tile)
            third_layer(last_tile)

        @block.vector
        def _(dve):
            def make_one_hot(t):
                for k in range(HOT):
                    wanted = hot_ids_sb[:, bass.ds(t, 1), k, :].to_broadcast([P, HOT_BLOCKS, TILE])
                    held = hot_row_sb.unsqueeze(2).to_broadcast([P, HOT_BLOCKS, TILE])
                    nc.vector.tensor_tensor(one_hot[:, k], wanted, held, ALU.is_equal).then_inc(one_hot_ready, 1)

            def take_away(k, part):
                return nc.vector.tensor_tensor(hot_rest[:, k], hot_rest[:, k], hot_split[part][:, k], ALU.subtract)

            def place_my_groups(t, h, groups):
                for g in groups:
                    if number(h, g) % 2 == 0:
                        dve.wait_ge(turned[h], t * len(GROUPS) + g + 1)
                        place_group(nc.vector.tensor_copy, h, g).then_inc(placed_dve, 1)

            def place_my_pairs(t, h):
                for u in range(UNITS):
                    dve.wait_ge(gram_done[u], t * 2 + h + 1)
                    place_pairs(nc.vector.tensor_copy, h, u, range(QUAD // 2)).then_inc(pairs_dve[u], 1)

            def first_units(t):
                dve.wait_ge(h1_sum[0], t + 1)
                for n in range(N1 // 2):
                    last = nc.vector.tensor_scalar(h1[:, n, :], ps_mlp[0][:, n * TILE:(n + 1) * TILE],
                                                   b1_sb[:, n:n + 1], 0.0, ALU.add, ALU.max)
                last.then_inc(h1_ready[0], 1)

            def second_units(t):
                dve.wait_ge(h2_sum[0], t + 1)
                nc.vector.tensor_scalar(h2[:, 0, :], ps_mlp[0][:, 0:TILE], b2_sb[:, 0:1], 0.0,
                                        ALU.add, ALU.max).then_inc(h2_ready[0], 1)

            def score(t):
                dve.wait_ge(y_sum, t + 1)
                nc.vector.tensor_copy(y_row[:, bass.ds(t * TILE, TILE)], ps_mlp[0][0:1, 0:TILE]).then_inc(y_ready, 1)

            def hot_rows(t):
                dve.wait_ge(hot_read, t)
                make_one_hot(t)

            def tile(t):
                place_my_groups(t, 0, [0])
                first_units(t - 1)
                place_my_groups(t, 0, [2])
                if not is_last(t):
                    hot_rows(t + 1)
                place_my_pairs(t, 0)
                second_units(t - 1)
                place_my_groups(t, 1, [1])
                score(t - 1)
                place_my_pairs(t, 1)

            for h in range(2):
                nc.vector.memset(features_t[h][:, :, FEATURES:SLOTS], 0.0).then_inc(slots_zeroed, 1)
            nc.vector.memset(pairs[P // 2:P, PAIR_TILES - 1, :], 0.0).then_inc(slots_zeroed, 1)
            dve.wait_ge(numbers_loaded, 16)
            nc.vector.tensor_tensor(rows[:, :, :], ids_sb,
                                    base_sb.unsqueeze(1).to_broadcast([P, TILES * 2, GATHERS]),
                                    ALU.add).then_inc(rows_ready, 1)
            dve.wait_ge(hot_ids_loaded[0], 16)
            make_one_hot(0)
            for step in range(HOT + 1):
                if step == HOT - 1:
                    place_my_groups(0, 0, [0])
                if step < HOT:
                    dve.wait_ge(split_ready[0], step + 1)
                    take_away(step, 0).then_inc(rest_ready, 1)
                if step >= 1:
                    dve.wait_ge(split_ready[1], step)
                    nc.vector.tensor_tensor(hot_split[2][:, step - 1], hot_rest[:, step - 1],
                                            hot_split[1][:, step - 1], ALU.subtract).then_inc(split_ready[2], 1)
            place_my_groups(0, 0, [2])
            dve.wait_ge(hot_ids_loaded[1], 16)
            hot_rows(1)
            place_my_pairs(0, 0)
            place_my_groups(0, 1, [1])
            dve.wait_ge(w_dense_loaded, 32)
            nc.vector.tensor_tensor(w_dense[:, :], w_dense_in[:, 0, :], w_dense_in[:, 1, :],
                                    ALU.add).then_inc(w_dense_ready, 1)
            place_my_pairs(0, 1)
            dve.wait_ge(bias_loaded, 32)
            dve.wait_ge(hot_ids_loaded[2], 16)
            with dve.Fori(1, last_tile) as t:
                tile(t)
            tile(last_tile)
            first_units(last_tile)
            second_units(last_tile)
            score(last_tile)

        @block.scalar
        def _(act):
            def keep_hot(t):
                act.wait_ge(hot_read, t + 1)
                nc.scalar.copy(kept[:, 1:KEPT, bass.ds(t * TILE, TILE)],
                               ps_mlp[1][:, :].rearrange("p (f s) -> p f s", s=TILE)).then_inc(hot_kept, 1)

            def place_my_groups(t, h, groups):
                for g in groups:
                    if number(h, g) % 2 == 1:
                        act.wait_ge(turned[h], t * len(GROUPS) + g + 1)
                        place_group(nc.scalar.copy, h, g).then_inc(placed_act, 1)

            def place_kept(t, h):
                act.wait_ge(turned[h], t * len(GROUPS) + 1)
                act.wait_ge(hot_kept, t + 1)
                nc.scalar.copy(features_t[h][:, :, 0:KEPT],
                               kept[:, :, bass.ds(t * TILE + h * HALF, HALF)].rearrange("p f s -> p s f")
                               ).then_inc(kept_placed, 1)

            def place_my_pairs(t, h):
                for u in range(UNITS):
                    act.wait_ge(gram_done[u], t * 2 + h + 1)
                    place_pairs(nc.scalar.copy, h, u, range(QUAD // 2, QUAD)).then_inc(pairs_act[u], 1)

            def first_units(t):
                act.wait_ge(h1_sum[1], t + 1)
                for n in range(N1 // 2, N1):
                    last = nc.scalar.activation(h1[:, n, :], ps_mlp[1][:, (n % 2) * TILE:(n % 2 + 1) * TILE],
                                                ACT.Relu, bias=b1_sb[:, n:n + 1])
                last.then_inc(h1_ready[1], 1)

            def second_units(t):
                act.wait_ge(h2_sum[1], t + 1)
                nc.scalar.activation(h2[:, 1, :], ps_mlp[1][:, 0:TILE], ACT.Relu,
                                     bias=b2_sb[:, 1:2]).then_inc(h2_ready[1], 1)

            def tile(t):
                place_kept(t, 0)
                place_my_groups(t, 0, [1])
                first_units(t - 1)
                place_my_pairs(t, 0)
                place_kept(t, 1)
                place_my_groups(t, 1, [0])
                second_units(t - 1)
                place_my_groups(t, 1, [2])
                if not is_last(t):
                    keep_hot(t + 1)
                place_my_pairs(t, 1)

            act.dma_start(hot_ids_sb[:, 0], hot_ids[:, 0]).then_inc(hot_ids_loaded[0], 16)
            act.dma_start(ident_sb[:, :], identity).then_inc(ident_loaded, 16)
            act.dma_start(kept[:, 0, :], dense_t).then_inc(dense_loaded, 16)
            for step in range(HOT + 1):
                if step < HOT:
                    act.wait_ge(hot_loaded[step], 16)
                    nc.scalar.copy(hot_split[0][:, step], hot_rest[:, step]).then_inc(split_ready[0], 1)
                if step >= 1:
                    act.wait_ge(rest_ready, step)
                    nc.scalar.copy(hot_split[1][:, step - 1], hot_rest[:, step - 1]).then_inc(split_ready[1], 1)
            place_my_groups(0, 0, [1])
            keep_hot(0)
            act.wait_ge(dense_loaded, 16)
            place_kept(0, 0)
            place_my_pairs(0, 0)
            place_kept(0, 1)
            place_my_groups(0, 1, [0, 2])
            keep_hot(1)
            place_my_pairs(0, 1)
            act.wait_ge(bias_loaded, 32)
            with act.Fori(1, last_tile) as t:
                tile(t)
            tile(last_tile)
            first_units(last_tile)
            second_units(last_tile)


def kernel(**inputs):
    import numpy as np
    import concourse.bacc as bacc
    from concourse.bass_utils import run_bass_kernel_spmd

    tables = [np.asarray(inputs[f"tbl_{f}"]) for f in range(SPARSE)]
    ids = np.asarray(inputs["ids"])
    w1 = np.asarray(inputs["W_top1"])
    assert [len(table) for table in tables] == TABLE_ROWS
    sizes = [TABLE_ROWS[f] for f in COLD_TABLES]
    first = np.array([sum(sizes[:k]) for k in range(len(sizes))], np.int32)

    ids_laid = ids[:, COLD_TABLES].reshape(TILES * 2, HALF, GATHERS, PER_GATHER).transpose(3, 1, 0, 2)
    base = np.repeat(first.reshape(GATHERS, PER_GATHER).T, HALF, axis=0)
    hot_row = np.arange(HOT_SPAN, dtype=np.int32).reshape(P, HOT_BLOCKS)
    hot_tables = np.zeros((HOT, HOT_SPAN, EMBED), tables[0].dtype)
    for k, f in enumerate(HOT_TABLES):
        hot_tables[k, :HOT_ROWS] = tables[f]
    hot_ids = ids[:, HOT_TABLES].reshape(TILES, TILE, HOT).transpose(0, 2, 1)
    slot = {0: 0} | {1 + f: 1 + i for i, f in enumerate(HOT_TABLES + COLD_TABLES)}
    w_pairs = np.zeros((QUAD, 32, PAIR_TILES, HIDDEN1), w1.dtype)
    at = EMBED
    for i in range(FEATURES):
        for j in range(i + 1, FEATURES):
            f, g = sorted((slot[i], slot[j]))
            w_pairs[(g - 1) % QUAD, f, (g - 1) // QUAD] = w1[at]
            at += 1
    arrays = {
        "table": np.concatenate([tables[f] for f in COLD_TABLES], axis=0),
        "numbers": np.concatenate([ids_laid.reshape(P, -1), base, hot_row], axis=1),
        "hot_tables": hot_tables.reshape(HOT, P, HOT_BLOCKS, EMBED),
        "hot_ids": np.broadcast_to(hot_ids, (P, TILES, HOT, TILE)),
        "dense_t": np.asarray(inputs["r_dense_features"]).T,
        "identity": np.eye(P, dtype=np.float32),
        "w_pairs": w_pairs.reshape(P, PAIR_TILES, HIDDEN1),
        "w_dense_a": w1[0:EMBED],
        "w_dense_b": w1[at:at + EMBED],
        "b_top1": np.asarray(inputs["b_top1"]).reshape(N1, P).T,
        "w_top2": np.asarray(inputs["W_top2"]).reshape(N1, P, HIDDEN2).transpose(1, 0, 2),
        "b_top2": np.asarray(inputs["b_top2"]).reshape(N2, P).T,
        "w_top3": np.asarray(inputs["W_top3"]).reshape(N2, P).T,
    }
    arrays = {name: np.ascontiguousarray(a) for name, a in arrays.items()}

    nc = bacc.Bacc("TRN2", target_bir_lowering=False, num_devices=1)
    args = {name: nc.dram_tensor(name, a.shape, mybir.dt.from_np(a.dtype), kind="ExternalInput").ap()
            for name, a in arrays.items()}
    out = nc.dram_tensor("out", (1, BATCH), F32, kind="ExternalOutput").ap()
    dlrm_tower(nc, out=out, **args)
    r = run_bass_kernel_spmd(nc, [arrays], core_ids=[0])
    return r.results[0]["out"].reshape(BATCH, 1)
```
